# Optimizing a Trainium2 kernel written in Bass

```python
import numpy as np
import jax
import jax.numpy as jnp

def _softmax(x, axis=-1):
    return jax.nn.softmax(x, axis=axis)

def _gelu(x):
    return jax.nn.gelu(x, approximate=True)

def _silu(x):
    return jax.nn.silu(x)

def _sigmoid(x):
    return jax.nn.sigmoid(x)

def _layernorm(x, axis=-1, eps=1e-05):
    m = jnp.mean(x, axis=axis, keepdims=True)
    v = jnp.var(x, axis=axis, keepdims=True)
    return (x - m) / jnp.sqrt(v + eps)

def _scatter_add(tgt, idx, src, axis=0):
    return tgt.at[idx].add(src)

def _segment_sum(src, seg, n):
    return jax.ops.segment_sum(src, seg, n)
kernel_name = 'mk_adaln_d1_jaxref_r8_c30d81'

def setup_inputs(seed: int=0):
    np.random.seed(seed)
    _w = jnp.asarray

    def _L0_attn_setup():
        import jax, jax.numpy as jnp
        import numpy as np
        NH = 16
        D = 128
        C = 64
        EPS = 1e-12

        def _l2norm(x):
            n = jnp.linalg.norm(x, axis=-1, keepdims=True)
            return x / jnp.maximum(n, EPS)
        key = jax.random.key(seed)
        ks = jax.random.split(key, 12)
        B, L, H = (4, 512, 256)
        std = 0.02
        f32 = jnp.float32
        inp = {'hidden_states': jax.random.normal(ks[0], (B, L, H), f32), 'q_w': jax.random.normal(ks[1], (NH * D, H), f32) * std, 'q_b': jnp.zeros((NH * D,), f32), 'k_w': jax.random.normal(ks[2], (NH * D, H), f32) * std, 'k_b': jnp.zeros((NH * D,), f32), 'v_w': jax.random.normal(ks[3], (NH * D, H), f32) * std, 'v_b': jnp.zeros((NH * D,), f32), 'a_w': jax.random.normal(ks[4], (NH, H), f32) * std, 'a_b': jnp.zeros((NH,), f32), 'b_w': jax.random.normal(ks[5], (NH, H), f32) * std, 'b_b': jnp.zeros((NH,), f32), 'og_w': jax.random.normal(ks[6], (NH * D, H), f32) * std, 'o_w': jax.random.normal(ks[7], (H, NH * D), f32) * std, 'o_b': jnp.zeros((H,), f32)}
        return inp
    _L0_attn_in = _L0_attn_setup()

    def _L0_ffn_setup():
        import jax, jax.numpy as jnp
        import numpy as np
        from jax import lax
        H = 256
        I = 176
        E = 16
        TOP_K = 6
        IS = 2 * I

        def _swiglu(x, w13_, w2_):
            gu = x @ w13_.T
            g, u = jnp.split(gu, 2, axis=-1)
            return jax.nn.silu(g) * u @ w2_.T
        key = jax.random.key(seed)
        ks = jax.random.split(key, 6)
        return {'hidden_states': jax.random.normal(ks[0], (1, 256, H), jnp.float32), 'gate_w': jax.random.normal(ks[1], (E, H), jnp.float32) * 0.02, 'w13': jax.random.normal(ks[2], (E, 2 * I, H), jnp.float32) * 0.02, 'w2': jax.random.normal(ks[3], (E, H, I), jnp.float32) * 0.02, 'sw13': jax.random.normal(ks[4], (2 * IS, H), jnp.float32) * 0.02, 'sw2': jax.random.normal(ks[5], (H, IS), jnp.float32) * 0.02}
    _L0_ffn_in = _L0_ffn_setup()
    _L0_c = _w((lambda *s: np.random.randn(*s).astype(np.float32) * 0.05)(16, 256))
    _L0_wmod = _w((lambda *s: np.random.randn(*s).astype(np.float32) * 0.05)(256, 6 * 256) * 256 ** (-0.5))
    _d = {'L0_attn_hidden_states': _L0_attn_in['hidden_states'], 'L0_attn_q_w': _L0_attn_in['q_w'], 'L0_attn_q_b': _L0_attn_in['q_b'], 'L0_attn_k_w': _L0_attn_in['k_w'], 'L0_attn_k_b': _L0_attn_in['k_b'], 'L0_attn_v_w': _L0_attn_in['v_w'], 'L0_attn_v_b': _L0_attn_in['v_b'], 'L0_attn_a_w': _L0_attn_in['a_w'], 'L0_attn_a_b': _L0_attn_in['a_b'], 'L0_attn_b_w': _L0_attn_in['b_w'], 'L0_attn_b_b': _L0_attn_in['b_b'], 'L0_attn_og_w': _L0_attn_in['og_w'], 'L0_attn_o_w': _L0_attn_in['o_w'], 'L0_attn_o_b': _L0_attn_in['o_b'], 'L0_ffn_gate_w': _L0_ffn_in['gate_w'], 'L0_ffn_w13': _L0_ffn_in['w13'], 'L0_ffn_w2': _L0_ffn_in['w2'], 'L0_ffn_sw13': _L0_ffn_in['sw13'], 'L0_ffn_sw2': _L0_ffn_in['sw2'], 'L0_c': _L0_c, 'L0_wmod': _L0_wmod}
    _x0 = _d['L0_attn_hidden_states']
    _d['L0_attn_hidden_states'] = jax.random.normal(jax.random.fold_in(jax.random.key(seed), 1), (16, 256, 256), dtype=_x0.dtype)
    del _x0
    return _d

def reference(L0_attn_hidden_states, L0_attn_q_w, L0_attn_q_b, L0_attn_k_w, L0_attn_k_b, L0_attn_v_w, L0_attn_v_b, L0_attn_a_w, L0_attn_a_b, L0_attn_b_w, L0_attn_b_b, L0_attn_og_w, L0_attn_o_w, L0_attn_o_b, L0_ffn_gate_w, L0_ffn_w13, L0_ffn_w2, L0_ffn_sw13, L0_ffn_sw2, L0_c, L0_wmod):

    def _L0_attn_ref(hidden_states, q_w, q_b, k_w, k_b, v_w, v_b, a_w, a_b, b_w, b_b, og_w, o_w, o_b):
        import jax, jax.numpy as jnp
        import numpy as np
        NH = 16
        D = 128
        C = 64
        EPS = 1e-12

        def _l2norm(x):
            n = jnp.linalg.norm(x, axis=-1, keepdims=True)
            return x / jnp.maximum(n, EPS)
        B, L, H = hidden_states.shape
        nh, d, c = (NH, D, C)
        hs = hidden_states
        q = (hs @ q_w.T + q_b).reshape(B, L, nh, d)
        k = (hs @ k_w.T + k_b).reshape(B, L, nh, d)
        v = (hs @ v_w.T + v_b).reshape(B, L, nh, d)
        beta = jax.nn.softplus(hs @ b_w.T + b_b)
        scale = float(d) ** 0.5
        qn = _l2norm(q / scale)
        kn = _l2norm(k / scale)
        gv = beta[..., None] * v
        nchunks = L // c

        def to_chunks(x):
            return x.reshape(B, nchunks, c, nh, d).transpose(0, 1, 3, 2, 4)
        qc, kc, gvc = (to_chunks(qn), to_chunks(kn), to_chunks(gv))
        attn = jnp.einsum('bnhid,bnhjd->bnhij', qc, kc)
        pos = jnp.arange(c, dtype=jnp.float32)
        dist = jnp.clip(pos[None, :] - pos[:, None], 0.0, None)
        decay = jnp.exp(-0.1 * dist)
        causal = pos[None, :] <= pos[:, None]
        mask = jnp.where(causal, decay, 0.0)
        out = jnp.einsum('bnhij,bnhjd->bnhid', attn * mask, gvc)
        out = out.transpose(0, 1, 3, 2, 4).reshape(B, L, nh * d)
        gate = jax.nn.silu(hs @ og_w.T)
        out = out * gate
        return out @ o_w.T + o_b

    def _L0_ffn_ref(hidden_states, gate_w, w13, w2, sw13, sw2):
        import jax, jax.numpy as jnp
        import numpy as np
        from jax import lax
        H = 256
        I = 176
        E = 16
        TOP_K = 6
        IS = 2 * I

        def _swiglu(x, w13_, w2_):
            gu = x @ w13_.T
            g, u = jnp.split(gu, 2, axis=-1)
            return jax.nn.silu(g) * u @ w2_.T
        B, S, Hd = hidden_states.shape
        x = hidden_states.reshape(-1, Hd)
        T = x.shape[0]
        scores = jax.nn.softmax(x @ gate_w.T, axis=-1)
        topk_w, topk_ids = lax.top_k(scores, TOP_K)
        topk_w = topk_w / (topk_w.sum(-1, keepdims=True) + 1e-20)
        combine = jnp.einsum('tk,tke->te', topk_w, jax.nn.one_hot(topk_ids, E, dtype=topk_w.dtype))

        def body(acc, ew):
            w13_e, w2_e, c_e = ew
            y = _swiglu(x, w13_e, w2_e)
            return (acc + c_e[:, None] * y, None)
        out, _ = lax.scan(body, jnp.zeros_like(x), (w13, w2, combine.T))
        out = out + _swiglu(x, sw13, sw2)
        return out.reshape(B, S, Hd)
    x = L0_attn_hidden_states
    mod = (_silu(L0_c) @ L0_wmod).reshape(L0_c.shape[0], 6, 1, -1)
    sa, ca, ga, sb, cb, gb = (mod[:, 0], mod[:, 1], mod[:, 2], mod[:, 3], mod[:, 4], mod[:, 5])
    ga = (2 * (ga >= 0) - 1) * jnp.maximum(jnp.abs(ga), 0.25)
    gb = (2 * (gb >= 0) - 1) * jnp.maximum(jnp.abs(gb), 0.25)
    h = _layernorm(x, axis=-1) * (1 + ca) + sa
    x = x + ga * _L0_attn_ref(h, L0_attn_q_w, L0_attn_q_b, L0_attn_k_w, L0_attn_k_b, L0_attn_v_w, L0_attn_v_b, L0_attn_a_w, L0_attn_a_b, L0_attn_b_w, L0_attn_b_b, L0_attn_og_w, L0_attn_o_w, L0_attn_o_b)
    h = _layernorm(x, axis=-1) * (1 + cb) + sb
    x = x + gb * _L0_ffn_ref(h, L0_ffn_gate_w, L0_ffn_w13, L0_ffn_w2, L0_ffn_sw13, L0_ffn_sw2)
    return x

_drawn_inputs = setup_inputs


def setup_inputs(seed=0):
    import zlib

    import numpy as np

    out = dict(_drawn_inputs(seed))
    spreads = {'L0_attn_q_b': (0.0, 0.8),
     'L0_attn_k_b': (0.0, 0.8),
     'L0_attn_v_b': (0.0, 0.8),
     'L0_attn_a_b': (0.0, 0.1),
     'L0_attn_b_b': (0.0, 0.8),
     'L0_attn_o_b': (0.0, 2.0)}
    factors = {'L0_attn_q_w': 8.0,
     'L0_attn_k_w': 8.0,
     'L0_attn_v_w': 8.0,
     'L0_attn_b_w': 8.0,
     'L0_attn_og_w': 8.0,
     'L0_attn_o_w': 8.0,
     'L0_ffn_gate_w': 8.0,
     'L0_ffn_w13': 8.0,
     'L0_ffn_w2': 8.0,
     'L0_ffn_sw13': 8.0,
     'L0_ffn_sw2': 8.0}
    for name, (base, spread) in spreads.items():
        noise = np.random.default_rng([zlib.crc32(name.encode()), seed]).standard_normal(out[name].shape)
        drawn = base * np.exp(spread * noise) if base else spread * noise
        out[name] = jnp.asarray(drawn.astype(out[name].dtype))
    for name, factor in factors.items():
        out[name] = (out[name] * factor).astype(out[name].dtype)
    return out
```

```python
import concourse.bass as bass
from concourse import mybir
from contextlib import ExitStack

FP32 = mybir.dt.float32
F32R = mybir.dt.float32r
ALU = mybir.AluOpType
ACT = mybir.ActivationFunctionType
AX = mybir.AxisListType

P = 128
H = 256
KC = H // P
B = 16
L = 256
T = B * L
NT = T // P
ST = 512
TS = ST // P
NS = T // ST
BS = ST // L
NH = 16
HG = 4
NG = NH // HG
CH = 64
E = 16
TOPK = 6
I = 176
IS = 2 * I
ER = P // E
ME = I // ER
MS = -(-IS // P)
NM = ME + MS
QKVW = 3 * H
HW_ = QKVW + 2 * H
MW = 3 * H
LN_EPS = 1e-5
NORM_EPS2 = (1e-12 * float(P) ** 0.5) ** 2
SA, CA, GA, SB, CB, GB = range(6)


def after(eng, sem, count):
    if isinstance(count, int) and count <= 0:
        return
    eng.wait_ge(sem, count)


def f32(ap):
    return ap.bitcast(FP32)


def heads(ap):
    return ap.rearrange("p (h d) -> p h d", d=P)


def one(ap, i, width=1):
    return ap[bass.ds(i, width)]


def prepare_weights(nc, q_w, k_w, v_w, og_w, o_w, w13, w2, sw13, sw2, ident, head_scr, tile_scr):
    ctx = ExitStack()
    with ctx:
        sb = lambda name, shape, dt=FP32: ctx.enter_context(nc.sbuf_tensor(name, shape, dt))
        sem = lambda name: ctx.enter_context(nc.semaphore(name))
        nat = [sb(f"w_nat{b}", [P, 5, H]) for b in range(2)]
        stage = [sb(f"w_stage{b}", [P, 2, HW_], F32R) for b in range(2)]
        bank = [[ctx.enter_context(nc.psum_tensor(f"w_bank{b}_{j}", [P, 512], FP32)) for j in range(3)]
                for b in range(2)]
        w2_nat = sb("w2_nat", [P, KC, E, I])
        w2_cols = [sb(f"w2_cols{b}", [P, KC, P]) for b in range(2)]
        sw2_nat = sb("sw2_nat", [P, KC, MS * P])
        loaded = [sem(f"w_loaded{b}") for b in range(2)]
        stored = [sem(f"w_stored{b}") for b in range(2)]
        w2_loaded, padded = sem("w2_loaded"), sem("w_padded")
        cols_copied = sem("w2_cols_copied")
        turned = sem("w_turned")
        hi_split, lo_split = sem("w_hi_split"), sem("w_lo_split")
        PARTS = [(0, 512), (512, 512), (1024, 256)]
        MPARTS = [(0, 512), (512, 256)]

        block = ctx.enter_context(nc.Block())

        @block.sync
        def _(sp):
            sp.dma_start(sw2_nat[:, :, 0:IS], sw2.rearrange("(c p) i -> p c i", p=P)).then_inc(w2_loaded, 16)
            for c in range(KC):
                sp.dma_start(w2_nat[:, c, :, :],
                             w2[:, c * P:(c + 1) * P, :].rearrange("e p i -> p e i")).then_inc(w2_loaded, 16)

            def load_head(r, b):
                for j, w in enumerate((q_w, k_w, v_w, og_w)):
                    sp.dma_start(nat[b][:, j, :], w[bass.ds(r * P, P), :]).then_inc(loaded[b], 16)
                sp.dma_start(nat[b][:, 4, :].rearrange("p (c n) -> p c n", c=KC),
                             o_w[:, bass.ds(r * P, P)].rearrange("(c p) n -> p c n", p=P)).then_inc(loaded[b], 16)

            def store_head(r, b):
                sp.wait_ge(hi_split, r + 1)
                sp.wait_ge(lo_split, r + 1)
                sp.dma_start(head_scr[bass.ds(r, 1)].rearrange("r s p n -> p (r s) n"),
                             f32(stage[b][:, :, :])).then_inc(stored[b], 16)

            load_head(0, 0)
            load_head(1, 1)
            with sp.Fori(0, NH // 2 - 1) as j:
                for b in range(2):
                    sp.wait_ge(turned, 2 * j + b + 1)
                    load_head(2 * j + b + 2, b)
                    store_head(2 * j + b, b)
            for b in range(2):
                store_head(NH - 2 + b, b)

            def load_tile(m, b):
                for j in range(2):
                    sp.dma_start(nat[b][:, j, :],
                                 w13[:, bass.ds(m * ER + j * I, ER), :]).then_inc(loaded[b], 16)

            def store_tile(m, b):
                sp.wait_ge(hi_split, NH + m + 1)
                sp.wait_ge(lo_split, NH + m + 1)
                sp.dma_start(tile_scr[bass.ds(m, 1)].rearrange("r p s n -> p (r s) n"),
                             f32(stage[b][:, :, 0:MW])).then_inc(stored[b], 16)

            for b in range(2):
                sp.wait_ge(turned, NH - 1 + b)
                load_tile(b, b)
            with sp.Fori(0, ME // 2 - 1) as j:
                for b in range(2):
                    sp.wait_ge(turned, NH + 2 * j + b + 1)
                    load_tile(2 * j + b + 2, b)
                    store_tile(2 * j + b, b)
            for b in range(2):
                store_tile(ME - 2 + b, b)
            for k in range(MS):
                m, b, n = ME + k, (ME + k) % 2, min(P, IS - k * P)
                sp.wait_ge(turned, NH + m - 1)
                if n < P:
                    sp.wait_ge(padded, 2)
                for j in range(2):
                    sp.dma_start(nat[b][0:n, j, :], sw13[j * IS + k * P:j * IS + k * P + n, :]).then_inc(loaded[b], 16)
                store_tile(m, b)
            for b in range(2):
                sp.wait_ge(stored[b], 16 * ((NH + NM + 1 - b) // 2))

        @block.gpsimd
        def _(pool):
            pool.memset(sw2_nat[:, :, IS:], 0.0).then_inc(padded, 1)
            pool.wait_ge(w2_loaded, 48)

            def copy_cols(m, b):
                after(pool, turned, NH + m - 1)
                pool.tensor_copy(w2_cols[b][:, :, :].rearrange("p c (e r) -> p c e r", e=E),
                                 w2_nat[:, :, :, bass.ds(m * ER, ER)]).then_inc(cols_copied, 1)

            for b in range(2):
                copy_cols(b, b)
            with pool.Fori(1, ME // 2) as j:
                for b in range(2):
                    copy_cols(2 * j + b, b)
            b = (NM - 1) % 2
            pool.wait_ge(turned, NH + NM - 2)
            pool.memset(nat[b][:, 0:2, :], 0.0).then_inc(padded, 1)

        @block.tensor
        def _(pe):
            def turn_head(r, use, b):
                after(pe, hi_split, r - 1)
                after(pe, lo_split, r - 1)
                pe.wait_ge(loaded[b], use * 80)
                for j in range(5):
                    for c in range(KC):
                        at = j * H + c * P
                        mm = pe.transpose(bank[b][at // 512][:, at % 512:at % 512 + P],
                                          nat[b][:, j, c * P:(c + 1) * P], ident)
                mm.then_inc(turned, 1)

            def turn_tile(m, loads, b):
                pe.wait_ge(hi_split, NH + m - 1)
                pe.wait_ge(lo_split, NH + m - 1)
                pe.wait_ge(loaded[b], loads)
                for j in range(2):
                    for c in range(KC):
                        at = j * H + c * P
                        pe.transpose(bank[b][0][:, at:at + P], nat[b][:, j, c * P:(c + 1) * P], ident)
                if isinstance(m, int) and m >= ME:
                    k = m - ME
                    pe.wait_ge(padded, 1)
                    cols = [sw2_nat[:, c, k * P:(k + 1) * P] for c in range(KC)]
                else:
                    pe.wait_ge(cols_copied, m + 1)
                    cols = [w2_cols[b][:, c, :] for c in range(KC)]
                for c in range(KC):
                    mm = pe.transpose(bank[b][1][:, c * P:(c + 1) * P], cols[c], ident)
                mm.then_inc(turned, 1)

            for b in range(2):
                turn_head(b, 1, b)
            with pe.Fori(1, NH // 2) as j:
                for b in range(2):
                    turn_head(2 * j + b, j + 1, b)
            with pe.Fori(0, ME // 2) as j:
                for b in range(2):
                    turn_tile(2 * j + b, 80 * (NH // 2) + 32 * (j + 1), b)
            for m in range(ME, NM):
                turn_tile(m, 80 * (NH // 2) + 32 * (m // 2 + 1), m % 2)

        def split(eng, do, done):
            def head(r, uses, b):
                eng.wait_ge(turned, r + 1)
                after(eng, stored[b], uses)
                do(b, PARTS, r)

            for b in range(2):
                head(b, 0, b)
            with eng.Fori(1, NH // 2) as j:
                for b in range(2):
                    head(2 * j + b, 16 * j, b)
            with eng.Fori(0, ME // 2) as j:
                for b in range(2):
                    eng.wait_ge(turned, NH + 2 * j + b + 1)
                    eng.wait_ge(stored[b], 8 * NH + 16 * j)
                    do(b, MPARTS, NH + 2 * j + b)
            for m in range(ME, NM):
                eng.wait_ge(turned, NH + m + 1)
                eng.wait_ge(stored[m % 2], 8 * NH + 16 * (m // 2))
                do(m % 2, MPARTS, NH + m)

        @block.scalar
        def _(act):
            def hi(b, parts, u):
                for j, (at, n) in enumerate(parts):
                    x = act.activation(stage[b][:, 0, at:at + n], bank[b][j][:, 0:n], ACT.Copy)
                x.then_inc(hi_split, 1)

            split(act, hi, hi_split)

        @block.vector
        def _(dve):
            def lo(b, parts, u):
                dve.wait_ge(hi_split, u + 1)
                for j, (at, n) in enumerate(parts):
                    x = dve.tensor_tensor(stage[b][:, 1, at:at + n], bank[b][j][:, 0:n],
                                          f32(stage[b][:, 0, at:at + n]), ALU.subtract)
                x.then_inc(lo_split, 1)

            split(dve, lo, lo_split)


def modulation(nc, c, wmod, o_b, b_w, gate_w, b_b, ident, k):
    ctx = ExitStack()
    with ctx:
        sb = lambda name, shape: ctx.enter_context(nc.sbuf_tensor(name, shape, FP32))
        pb = lambda name: ctx.enter_context(nc.psum_tensor(name, [P, 512], FP32))
        sem = lambda name: ctx.enter_context(nc.semaphore(name))
        narrow = sb("narrow", [B, 3, H])
        silu_c = sb("silu_c", [B, H])
        wmod_sb = sb("wmod_sb", [P, KC, 6 * H])
        silu_t = sb("silu_t", [P, KC, B])
        turned_ps, mod_ps = pb("m_turned_ps"), pb("m_mod_ps")
        loaded, c_ready, t_ready, t_copied = sem("m_loaded"), sem("m_silu"), sem("m_turned"), sem("m_copied")
        mod_ready, gained = sem("m_mod"), sem("m_gained")
        parts = mod_ps[:, 0:6 * KC * B].rearrange("p (w b) -> p w b", b=B)
        block = ctx.enter_context(nc.Block())

        @block.sync
        def _(sp):
            for j, src in enumerate((c, b_w, gate_w)):
                sp.dma_start(narrow[:, j, :], src).then_inc(loaded, 16)
            sp.dma_start(wmod_sb[:, :, :], wmod.rearrange("(c p) n -> p c n", p=P)).then_inc(loaded, 16)
            sp.dma_start(k.o_b[:, :], o_b.rearrange("(c p) -> p c", p=P),
                         allow_slow_non_contiguous=True).then_inc(loaded, 16)
            sp.dma_start(k.b_b[:, :], b_b.rearrange("(a n) -> a n", a=1).partition_broadcast(P)
                         .rearrange("p a n -> p (a n)")).then_inc(loaded, 16)
            sp.wait_ge(loaded, 96)

        @block.scalar
        def _(act):
            act.wait_ge(loaded, 96)
            act.activation(silu_c[:, :], narrow[:, 0, :], ACT.Silu).then_inc(c_ready, 1)

        @block.tensor
        def _(pe):
            pe.wait_ge(c_ready, 1)
            for j in range(3):
                for h in range(KC):
                    src = silu_c[:, h * P:(h + 1) * P] if j == 0 else narrow[:, j, h * P:(h + 1) * P]
                    at = (j * KC + h) * B
                    mm = pe.transpose(turned_ps[:, at:at + B], src, ident[0:B, 0:B])
            mm.then_inc(t_ready, 1)
            pe.wait_ge(t_copied, 1)
            for w in range(6 * KC):
                for h in range(KC):
                    mm = pe.matmul(parts[:, w, :], wmod_sb[:, h, w * P:(w + 1) * P], silu_t[:, h, :],
                                   start=(h == 0), stop=(h == KC - 1))
            mm.then_inc(mod_ready, 1)

        @block.vector
        def _(dve):
            dve.wait_ge(t_ready, 1)
            n = KC * B
            dve.tensor_copy(silu_t[:, :, :].rearrange("p c b -> p (c b)"), turned_ps[:, 0:n]).then_inc(t_copied, 1)
            dve.tensor_copy(k.b_wt[:, :, :].rearrange("p c b -> p (c b)"), turned_ps[:, n:2 * n])
            dve.tensor_copy(k.gate_wt[:, :, :].rearrange("p c b -> p (c b)"), turned_ps[:, 2 * n:3 * n])
            dve.wait_ge(mod_ready, 1)
            dve.tensor_copy(k.mod[:, :, :], parts).then_inc(gained, 1)
            dve.wait_ge(gained, 1)
            steps = 1
            for w in (CA, CB):
                m = k.mod[:, w * KC:(w + 1) * KC, :]
                dve.tensor_scalar(m, m, 1.0, None, ALU.add).then_inc(gained, 1)
                steps += 1
            for w in (GA, GB):
                m, s = k.mod[:, w * KC:(w + 1) * KC, :], k.sign[:, :, :]
                dve.wait_ge(gained, steps)
                dve.tensor_scalar(s, m, 0.0, 2.0, ALU.is_ge, ALU.mult).then_inc(gained, 1)
                dve.wait_ge(gained, steps + 1)
                dve.scalar_tensor_tensor(out=m, in0=m, scalar=-1.0, in1=m, op0=ALU.mult, op1=ALU.max)\
                   .then_inc(gained, 1)
                dve.wait_ge(gained, steps + 2)
                dve.tensor_scalar(m, m, 0.25, None, ALU.max).then_inc(gained, 1)
                dve.wait_ge(gained, steps + 3)
                dve.scalar_tensor_tensor(out=m, in0=s, scalar=-1.0, in1=m, op0=ALU.add, op1=ALU.mult)\
                   .then_inc(gained, 1)
                steps += 4
            dve.wait_ge(gained, steps)
            for h in range(KC):
                dve.tensor_scalar(k.ga_ob[:, h, :], k.mod[:, GA * KC + h, :], k.o_b[:, h:h + 1], None, ALU.mult)\
                   .then_inc(gained, 1)
            dve.wait_ge(gained, steps + KC)


def normalize_inputs(nc, x, ident, k, h_scr):
    ctx = ExitStack()
    with ctx:
        sb = lambda name, shape, dt=FP32: ctx.enter_context(nc.sbuf_tensor(name, shape, dt))
        sem = lambda name: ctx.enter_context(nc.semaphore(name))
        x_in = [sb(f"n_x{b}", [P, TS, H]) for b in range(2)]
        stats = [sb(f"n_stats{b}", [P, TS, 6]) for b in range(2)]
        mean_var = [sb(f"n_mean_var{b}", [P, TS, 2]) for b in range(2)]
        var_eps = [sb(f"n_var_eps{b}", [P, TS]) for b in range(2)]
        rstd = [sb(f"n_rstd{b}", [P, TS]) for b in range(2)]
        xn = [sb(f"n_xn{b}", [P, TS, H]) for b in range(2)]
        h_f = [sb(f"n_h{b}", [P, KC, TS, P]) for b in range(2)]
        stage = [sb(f"n_stage{b}", [P, TS, 2, KC, P], F32R) for b in range(2)]
        z_all = sb("z_all", [P, NT * NH])
        soft = [sb(f"n_soft{j}", [P, NT * NH]) for j in range(3)]
        turned_ps = [[ctx.enter_context(nc.psum_tensor(f"n_turned{b}_{c}", [P, 512], FP32)) for c in range(KC)]
                     for b in range(2)]
        beta_ps = [ctx.enter_context(nc.psum_tensor(f"n_beta{b}", [P, 512], FP32)) for b in range(2)]
        loaded = [sem(f"n_loaded{b}") for b in range(2)]
        stored = [sem(f"n_stored{b}") for b in range(2)]
        stats_done, aggregated, eps_added, rstd_done = sem("n_st"), sem("n_ag"), sem("n_ep"), sem("n_rs")
        xn_done, turned, modulated = sem("n_xn"), sem("n_turned"), sem("n_mod")
        hi_done, lo_done, beta_done, z_done, softened = (sem("n_hi"), sem("n_lo"), sem("n_beta"), sem("n_z"),
                                                         sem("n_soft"))
        x_t = x.rearrange("b (a p) c -> (b a) p c", p=P)
        block = ctx.enter_context(nc.Block())

        @block.sync
        def _(sp):
            def load(s, b):
                sp.dma_start(x_in[b][:, :, :], x_t[bass.ds(s * TS, TS)].rearrange("t p c -> p t c"))\
                  .then_inc(loaded[b], 16)

            def store(s, b):
                sp.wait_ge(hi_done, s + 1)
                sp.wait_ge(lo_done, s + 1)
                sp.dma_start(h_scr[bass.ds(s * TS, TS)].rearrange("t p n -> p t n"),
                             f32(stage[b][:, :, :, :, :]).rearrange("p t s c n -> p t (s c n)")).then_inc(stored[b], 16)

            load(0, 0)
            load(1, 1)
            with sp.Fori(0, NS // 2 - 1) as j:
                for b in range(2):
                    s = 2 * j + b
                    sp.wait_ge(xn_done, s + 1)
                    load(s + 2, b)
                    store(s, b)
            for b in range(2):
                store(NS - 2 + b, b)
            for b in range(2):
                sp.wait_ge(stored[b], 16 * (NS // 2))

        @block.vector
        def _(dve):
            def measure(s, use, b):
                dve.wait_ge(loaded[b], 16 * use)
                after(dve, xn_done, s - 1)
                for t in range(TS):
                    i = dve.bn_stats(stats[b][:, t, :], x_in[b][:, t, :])
                i.then_inc(stats_done, 1)

            def normalize(s, b):
                dve.wait_ge(rstd_done, s + 1)
                after(dve, turned, s - 1)
                for t in range(TS):
                    i = dve.tensor_scalar(xn[b][:, t, :], x_in[b][:, t, :], mean_var[b][:, t, 0:1],
                                          rstd[b][:, t:t + 1], ALU.subtract, ALU.mult)
                i.then_inc(xn_done, 1)

            def aggregate(s, b):
                for t in range(TS):
                    i = dve.bn_aggr(mean_var[b][:, t, :], stats[b][:, t, :])
                i.then_inc(aggregated, 1)
                dve.wait_ge(aggregated, s + 1)
                after(dve, rstd_done, s - 1)
                dve.tensor_scalar(var_eps[b][:, :], mean_var[b][:, :, 1], LN_EPS, None, ALU.add).then_inc(eps_added, 1)

            def finish(s, b):
                dve.wait_ge(hi_done, s + 1)
                for c in range(KC):
                    i = dve.tensor_tensor(stage[b][:, :, 1, c, :], h_f[b][:, c, :, :], f32(stage[b][:, :, 0, c, :]),
                                          ALU.subtract)
                i.then_inc(lo_done, 1)
                dve.wait_ge(beta_done, s + 1)
                z = z_all[:, bass.ds(s * TS * NH, TS * NH)].rearrange("p (t h) -> p t h", h=NH)
                dve.tensor_tensor(z, beta_ps[b][:, 0:TS * NH].rearrange("p (t h) -> p t h", h=NH),
                                  k.b_b[:, :].unsqueeze(1).broadcast_to([P, TS, NH]), ALU.add).then_inc(z_done, 1)

            for s in range(2):
                measure(s, 1, s)
                dve.wait_ge(stats_done, s + 1)
                aggregate(s, s)
            normalize(0, 0)

            def pair(j):
                for b in range(2):
                    s = 2 * j + b
                    measure(s + 2, j + 2, b)
                    dve.wait_ge(stats_done, s + 3)
                    normalize(s + 1, 1 - b)
                    aggregate(s + 2, b)
                    finish(s, b)

            pair(0)
            with dve.Fori(1, NS // 2 - 1) as j:
                pair(j)
            normalize(NS - 1, 1)
            finish(NS - 2, 0)
            finish(NS - 1, 1)
            dve.wait_ge(z_done, NS)
            dve.scalar_tensor_tensor(out=soft[0][:, :], in0=z_all[:, :], scalar=-1.0, in1=z_all[:, :],
                                     op0=ALU.mult, op1=ALU.min).then_inc(softened, 1)
            dve.wait_ge(softened, 2)
            dve.tensor_scalar(soft[0][:, :], soft[1][:, :], 1.0, None, ALU.add).then_inc(softened, 1)
            dve.wait_ge(softened, 4)
            dve.scalar_tensor_tensor(out=soft[1][:, :], in0=soft[0][:, :], scalar=-1.0, in1=soft[1][:, :],
                                     op0=ALU.add, op1=ALU.subtract).then_inc(softened, 1)
            dve.wait_ge(softened, 5)
            dve.reciprocal(soft[0][:, :], soft[0][:, :]).then_inc(softened, 1)
            dve.wait_ge(softened, 6)
            dve.tensor_tensor(soft[1][:, :], soft[1][:, :], soft[0][:, :], ALU.mult).then_inc(softened, 1)
            dve.wait_ge(softened, 7)
            dve.tensor_tensor(soft[2][:, :], soft[2][:, :], soft[1][:, :], ALU.subtract).then_inc(softened, 1)
            dve.wait_ge(softened, 8)
            dve.scalar_tensor_tensor(out=k.beta[:, :, :].rearrange("p t h -> p (t h)"), in0=z_all[:, :], scalar=0.0,
                                     in1=soft[2][:, :], op0=ALU.max, op1=ALU.add).then_inc(softened, 1)
            dve.wait_ge(softened, 9)

        @block.gpsimd
        def _(pool):
            def root(s, b):
                pool.wait_ge(eps_added, s + 1)
                after(pool, xn_done, s - 1)
                pool.tensor_tensor(rstd[b][:, :], var_eps[b][:, :], k.minus_half[:, 0:TS], ALU.pow)\
                    .then_inc(rstd_done, 1)

            root(0, 0)
            root(1, 1)
            with pool.Fori(1, NS // 2) as j:
                for b in range(2):
                    root(2 * j + b, b)

        @block.tensor
        def _(pe):
            def turn(s, b):
                pe.wait_ge(xn_done, s + 1)
                after(pe, modulated, s - 1)
                for c in range(KC):
                    for t in range(TS):
                        mm = pe.transpose(turned_ps[b][c][:, t * P:(t + 1) * P], xn[b][:, t, c * P:(c + 1) * P], ident)
                mm.then_inc(turned, 1)

            def project(s, b):
                pe.wait_ge(modulated, s + 1)
                after(pe, z_done, s - 1)
                for t in range(TS):
                    for c in range(KC):
                        mm = pe.matmul(beta_ps[b][:, t * NH:(t + 1) * NH], h_f[b][:, c, t, :], k.b_wt[:, c, :],
                                       start=(c == 0), stop=(c == KC - 1))
                mm.then_inc(beta_done, 1)

            def both(s, b):
                turn(s, b)
                project(s, b)

            both(0, 0)
            both(1, 1)
            with pe.Fori(1, NS // 2) as j:
                for b in range(2):
                    both(2 * j + b, b)

        @block.scalar
        def _(act):
            def modulate(s, use, b):
                act.wait_ge(turned, s + 1)
                after(act, lo_done, s - 1)
                after(act, beta_done, s - 1)
                for c in range(KC):
                    for j in range(BS):
                        n = TS // BS
                        at = s * BS + j
                        i = act.activation(h_f[b][:, c, j * n:(j + 1) * n, :].rearrange("p t n -> p (t n)"),
                                           turned_ps[b][c][:, j * L:(j + 1) * L], ACT.Identity,
                                           bias=k.mod[:, SA * KC + c, bass.ds(at, 1)],
                                           scale=k.mod[:, CA * KC + c, bass.ds(at, 1)])
                i.then_inc(modulated, 1)
                act.wait_ge(modulated, s + 1)
                after(act, stored[b], 16 * use)
                for c in range(KC):
                    i = act.activation(stage[b][:, :, 0, c, :], h_f[b][:, c, :, :], ACT.Copy)
                i.then_inc(hi_done, 1)

            modulate(0, 0, 0)
            modulate(1, 0, 1)
            with act.Fori(1, NS // 2) as j:
                for b in range(2):
                    modulate(2 * j + b, j, b)
            act.wait_ge(softened, 1)
            act.activation(soft[1][:, :], soft[0][:, :], ACT.Exp).then_inc(softened, 1)
            act.wait_ge(softened, 3)
            act.activation(soft[2][:, :], soft[0][:, :], ACT.Ln).then_inc(softened, 1)


def attention(nc, q_b, k_b, v_b, ident, k, head_scr, h_scr, acc):
    ctx = ExitStack()
    with ctx:
        sb = lambda name, shape, dt=FP32: ctx.enter_context(nc.sbuf_tensor(name, shape, dt))
        pb = lambda name: ctx.enter_context(nc.psum_tensor(name, [P, 512], FP32))
        sem = lambda name: ctx.enter_context(nc.semaphore(name))
        N = NG * NS
        w_qkv = sb("w_qkv", [P, 2, HG, 2, QKVW], F32R)
        w_gate = sb("w_gate", [P, HG, 2, H], F32R)
        w_out = sb("w_out", [P, HG, 2, H], F32R)
        h_t = sb("h_t", [P, TS, 2, KC, P], F32R)
        bias = sb("a_bias", [P, 3, NH * P])
        raw = [[sb(f"{n}_sb{b}", [P, HG * P]) for b in range(2)] for n in "qkv"]
        squares = sb("squares", [P, 2, HG * P])
        sumsq = [sb(f"sumsq{b}", [P, 2 * HG]) for b in range(2)]
        guarded = [sb(f"guarded{b}", [P, 2 * HG]) for b in range(2)]
        inv_norm = [sb(f"inv_norm{b}", [P, 2 * HG]) for b in range(2)]
        v_scale = [sb(f"v_scale{b}", [P, HG]) for b in range(2)]
        q_t, k_t = sb("q_t", [P, HG * P]), sb("k_t", [P, HG * P])
        scores = sb("scores", [P, HG * P])
        gate = sb("gate", [P, HG, ST])
        gated = [sb(f"gated{b}", [P, HG, P]) for b in range(2)]
        gated_hi = sb("gated_hi", [P, 2, HG, ST], F32R)
        gated_lo = sb("gated_lo", [P, 2, HG, ST], F32R)
        proj_ps = [pb("proj_ps0"), pb("proj_ps1")]
        qt_ps, kt_ps, s_ps, av_ps = pb("qt_ps"), pb("kt_ps"), pb("s_ps"), pb("av_ps")
        out_ps = [pb(f"out_ps{c}") for c in range(KC)]

        qkv_loaded, gate_w_loaded, out_w_loaded, bias_loaded = (sem("qkv_loaded"), sem("gate_w_loaded"),
                                                                sem("out_w_loaded"), sem("bias_loaded"))
        h_loaded = [sem(f"h_loaded{t}") for t in range(TS)]
        projected = [sem(f"{n}_projected") for n in "qkv"]
        biased = [sem(f"{n}_biased") for n in "qkv"]
        gate_projected, gate_ready = sem("gate_projected"), sem("gate_ready")
        q_squared, k_squared, summed, guard_done, inverted = (sem("q_squared"), sem("k_squared"), sem("summed"),
                                                              sem("guard_done"), sem("inverted"))
        q_scaled, scale_done, v_scaled = sem("q_scaled"), sem("v_scale_done"), sem("v_scaled")
        q_turned, k_turned, qt_copied, kt_copied = sem("q_turned"), sem("k_turned"), sem("qt_copied"), sem("kt_copied")
        scored, masked, attended, gated_done = sem("scored"), sem("masked"), sem("attended"), sem("gated_done")
        hi_done, lo_done = sem("gated_hi_done"), sem("gated_lo_done")
        out_projected = [sem(f"out_projected{c}") for c in range(KC)]
        added = [sem(f"added{c}") for c in range(KC)]
        Q, K, V = range(3)

        ORDER = [(w, 0) for w in (Q, K, V)] + [("gate", h) for h in range(HG)] + \
                [(w, t) for t in range(1, TS) for w in (Q, K, V)]

        def bank_of(what, t):
            return proj_ps[ORDER.index((what, t)) % 2]

        def bank_free(eng, i, what, t):
            at = ORDER.index((what, t)) - 2
            before, u = ORDER[at]
            j = i if at >= 0 else i - 1
            if before == "gate":
                after(eng, gate_ready, HG * j + u + 1)
            else:
                after(eng, biased[before], TS * j + u + 1)

        def iterations(eng, run, last=True):
            run(0)
            with eng.Fori(1, N) as i:
                run(i)

        block = ctx.enter_context(nc.Block())

        @block.sync
        def _(sp):
            for j, src in enumerate((q_b, k_b, v_b)):
                sp.dma_start(bias[:, j, :], src.rearrange("(a n) -> a n", a=1).partition_broadcast(P)
                             .rearrange("p a n -> p (a n)")).then_inc(bias_loaded, 16)

            def load_h(n, t):
                sp.dma_start(f32(h_t[:, t, :, :, :]).rearrange("p s c n -> p (s c n)"),
                             h_scr[bass.ds(n, 1)].rearrange("t p n -> (t p) n")).then_inc(h_loaded[t], 16)

            def load_qkv(g):
                sp.dma_start(f32(w_qkv[:, g % 2, :, :, :]).rearrange("p h s n -> p (h s) n"),
                             head_scr[g * HG:(g + 1) * HG, :, :, 0:QKVW].rearrange("h s p n -> p (h s) n"))\
                  .then_inc(qkv_loaded, 16)

            def load_gate(g):
                sp.dma_start(f32(w_gate[:, :, :, :]).rearrange("p h s n -> p (h s) n"),
                             head_scr[g * HG:(g + 1) * HG, :, :, QKVW:QKVW + H].rearrange("h s p n -> p (h s) n"))\
                  .then_inc(gate_w_loaded, 16)

            def load_out(g):
                sp.dma_start(f32(w_out[:, :, :, :]).rearrange("p h s n -> p (h s) n"),
                             head_scr[g * HG:(g + 1) * HG, :, :, QKVW + H:HW_].rearrange("h s p n -> p (h s) n"))\
                  .then_inc(out_w_loaded, 16)

            def refill(i, s_next, t):
                if t == 0:
                    sp.wait_ge(gate_projected, HG * (i + 1))
                sp.wait_ge(projected[V], TS * i + t + 1)
                load_h(s_next * TS + t, t)

            load_qkv(0)
            for t in range(TS):
                load_h(t, t)
            load_gate(0)
            load_out(0)
            for g in range(NG):
                first = g * NS
                for t in range(TS):
                    refill(first, 1, t)
                if g > 0:
                    sp.wait_ge(out_projected[KC - 1], first)
                    load_out(g)
                if g + 1 < NG:
                    sp.wait_ge(qkv_loaded, 16 * (g + 1))
                    load_qkv(g + 1)
                with sp.Fori(1, NS - 1) as s:
                    for t in range(TS):
                        refill(first + s, s + 1, t)
                if g + 1 < NG:
                    last = first + NS - 1
                    for t in range(TS):
                        refill(last, 0, t)
                        if t == 0:
                            load_gate(g + 1)

        @block.tensor
        def _(pe):
            def split_product(out, pairs):
                n = 3 * len(pairs)
                for j, ((w_hi, w_lo), (x_hi, x_lo)) in enumerate(pairs):
                    for m, (w, y) in enumerate(((w_hi, x_hi), (w_lo, x_hi), (w_hi, x_lo))):
                        mm = pe.matmul(out, w, y, start=(j == 0 and m == 0), stop=(3 * j + m == n - 1))
                return mm

            def project(i, t, what):
                g = i // NS
                if what == Q:
                    pe.wait_ge(h_loaded[t], 16 * (i + 1))
                    if t == 0:
                        pe.wait_ge(qkv_loaded, 16 * (g + 1))
                bank_free(pe, i, what, t)
                w = w_qkv[:, bass.ds(g % 2, 1), :, :, :].rearrange("p a h s n -> p (a h) s n")
                pairs = [([h_t[:, t, s, c, :] for s in range(2)],
                          [w[:, :, s, what * H + c * P:what * H + (c + 1) * P] for s in range(2)]) for c in range(KC)]
                split_product(heads(bank_of(what, t)[:, :]), pairs).then_inc(projected[what], 1)

            def project_gate(i, h):
                if h == 0:
                    for t in range(1, TS):
                        pe.wait_ge(h_loaded[t], 16 * (i + 1))
                    pe.wait_ge(gate_w_loaded, 16 * (i // NS + 1))
                bank_free(pe, i, "gate", h)
                pairs = [([w_gate[:, h, s, c * P:(c + 1) * P] for s in range(2)],
                          [h_t[:, :, s, c, :] for s in range(2)]) for c in range(KC)]
                split_product(heads(bank_of("gate", h)[:, :]), pairs).then_inc(gate_projected, 1)

            def turn(n, b):
                pe.wait_ge(q_scaled, n)
                after(pe, qt_copied, n - 1)
                for h in range(HG):
                    mm = pe.transpose(qt_ps[:, h * P:(h + 1) * P], raw[Q][b][:, h * P:(h + 1) * P], ident)
                mm.then_inc(q_turned, 1)
                pe.wait_ge(biased[K], n)
                after(pe, kt_copied, n - 1)
                for h in range(HG):
                    mm = pe.transpose(kt_ps[:, h * P:(h + 1) * P], raw[K][b][:, h * P:(h + 1) * P], ident)
                mm.then_inc(k_turned, 1)

            def score(n):
                pe.wait_ge(qt_copied, n)
                pe.wait_ge(kt_copied, n)
                after(pe, masked, n - 1)
                for h in range(HG):
                    at = slice(h * P, (h + 1) * P)
                    mm = pe.matmul(s_ps[:, at], k_t[:, at], q_t[:, at], start=True, stop=True)
                mm.then_inc(scored, 1)

            def attend(n, b):
                pe.wait_ge(masked, n)
                pe.wait_ge(v_scaled, n)
                after(pe, gated_done, n - 1)
                for h in range(HG):
                    at = slice(h * P, (h + 1) * P)
                    mm = pe.matmul(av_ps[:, at], raw[V][b][:, at], scores[:, at], start=True, stop=True)
                mm.then_inc(attended, 1)

            def project_out(i, c):
                if c == 0:
                    pe.wait_ge(hi_done, TS * i)
                    pe.wait_ge(lo_done, TS * i)
                    pe.wait_ge(out_w_loaded, 16 * ((i - 1) // NS + 1))
                pe.wait_ge(added[c], i)
                b = (i - 1) % 2
                pairs = [([w_out[:, h, s, c * P:(c + 1) * P] for s in range(2)],
                          [x[:, bass.ds(b, 1), h, :].rearrange("p a n -> p (a n)") for x in (gated_hi, gated_lo)])
                         for h in range(HG)]
                split_product(out_ps[c][:, :], pairs).then_inc(out_projected[c], 1)

            def run(i):
                first = isinstance(i, int) and i == 0
                for t in range(TS):
                    n = TS * i + t
                    b = (t - 1) % 2
                    before = not (first and t == 0)
                    project(i, t, Q)
                    if before:
                        turn(n, b)
                    project(i, t, K)
                    if before:
                        score(n)
                    project(i, t, V)
                    if before:
                        attend(n, b)
                    if t == 0:
                        for h in range(HG):
                            project_gate(i, h)
                    if t in (1, 2) and not first:
                        project_out(i, t - 1)

            iterations(pe, run)
            turn(TS * N, 1)
            score(TS * N)
            attend(TS * N, 1)
            for c in range(KC):
                project_out(N, c)

        @block.vector
        def _(dve):
            def add_bias(i, t, what):
                n = TS * i + t
                dve.wait_ge(projected[what], n + 1)
                after(dve, (q_turned, k_turned, attended)[what], n - 1)
                dve.tensor_tensor(raw[what][t % 2][:, :], bank_of(what, t)[:, :],
                                  bias[:, what, bass.ds((i // NS) * ST, ST)], ALU.add).then_inc(biased[what], 1)

            def mask(n):
                dve.wait_ge(scored, n)
                after(dve, attended, n - 1)
                dve.tensor_tensor(heads(scores[:, :]), heads(s_ps[:, :]),
                                  k.causal[:, :].unsqueeze(1).broadcast_to([P, HG, P]), ALU.mult).then_inc(masked, 1)

            def apply_gate(n, t, b):
                dve.wait_ge(attended, n)
                dve.wait_ge(gate_ready, HG * ((n - 1) // TS + 1))
                after(dve, hi_done, n - 2)
                after(dve, lo_done, n - 2)
                dve.tensor_tensor(gated[b][:, :, :], heads(av_ps[:, :]), gate[:, :, t * P:(t + 1) * P], ALU.mult)\
                   .then_inc(gated_done, 1)

            def sum_squares(n, b):
                dve.wait_ge(q_squared, n + 1)
                dve.wait_ge(k_squared, n + 1)
                after(dve, guard_done, n - 1)
                dve.tensor_reduce(sumsq[b][:, :], squares[:, :, :].rearrange("p a (h d) -> p (a h) d", d=P), AX.X,
                                  ALU.add).then_inc(summed, 1)
                dve.wait_ge(summed, n + 1)
                after(dve, inverted, n - 1)
                dve.tensor_scalar(guarded[b][:, :], sumsq[b][:, :], NORM_EPS2, None, ALU.max).then_inc(guard_done, 1)

            def lo_part(n, i, t, b):
                dve.wait_ge(hi_done, n)
                at = [bass.ds(i % 2, 1), slice(None), slice(t * P, (t + 1) * P)]
                hi, lo = (x[:, at[0], at[1], at[2]].rearrange("p a h n -> p (a h) n") for x in (gated_hi, gated_lo))
                if t == 0:
                    after(dve, added[KC - 1], i)
                dve.tensor_tensor(lo, gated[b][:, :, :], f32(hi), ALU.subtract).then_inc(lo_done, 1)

            def add_out(i, c):
                dve.wait_ge(out_projected[c], i)
                dve.wait_ge(added[c], i)
                sums = acc[:, c, bass.ds(((i - 1) % NS) * ST, ST)]
                dve.tensor_tensor(sums, out_ps[c][:, :], sums, ALU.add).then_inc(added[c], 1)

            def run(i):
                first = isinstance(i, int) and i == 0
                for t in range(TS):
                    n = TS * i + t
                    tp, ip = (t - 1) % TS, i if t > 0 else i - 1
                    before = not (first and t == 0)
                    add_bias(i, t, Q)
                    add_bias(i, t, K)
                    if before:
                        mask(n)
                    sum_squares(n, t % 2)
                    add_bias(i, t, V)
                    if before:
                        apply_gate(n, tp, tp % 2)
                    if before:
                        lo_part(n, ip, tp, tp % 2)
                    if t in (2, 3) and not first:
                        add_out(i, t - 2)

            dve.wait_ge(bias_loaded, 48)
            for c in range(KC):
                dve.memset(acc[:, c, :], 0.0).then_inc(added[c], 1)
            iterations(dve, run)
            n = TS * N
            mask(n)
            apply_gate(n, TS - 1, 1)
            lo_part(n, N - 1, TS - 1, 1)
            for c in range(KC):
                add_out(N, c)

        @block.scalar
        def _(act):
            def copy_turned(n):
                act.wait_ge(q_turned, n)
                after(act, scored, n - 1)
                act.activation(q_t[:, :], qt_ps[:, :], ACT.Copy).then_inc(qt_copied, 1)
                act.wait_ge(k_turned, n)
                act.activation(k_t[:, :], kt_ps[:, :], ACT.Copy).then_inc(kt_copied, 1)

            def square(n, what, b):
                act.wait_ge(biased[what], n + 1)
                after(act, summed, n)
                act.activation(squares[:, what, :], raw[what][b][:, :], ACT.Square)\
                   .then_inc((q_squared, k_squared)[what], 1)

            def hi_part(n, i, t, b):
                act.wait_ge(gated_done, n)
                if t == 0:
                    after(act, added[KC - 1], i)
                act.activation(gated_hi[:, bass.ds(i % 2, 1), :, t * P:(t + 1) * P].rearrange("p a h n -> p (a h) n"),
                               gated[b][:, :, :], ACT.Copy).then_inc(hi_done, 1)

            def silu_gate(i, h):
                act.wait_ge(gate_projected, HG * i + h + 1)
                after(act, gated_done, TS * i)
                act.activation(gate[:, h, :], bank_of("gate", h)[:, :], ACT.Silu).then_inc(gate_ready, 1)

            def run(i):
                first = isinstance(i, int) and i == 0
                for t in range(TS):
                    n = TS * i + t
                    tp, ip = (t - 1) % TS, i if t > 0 else i - 1
                    before = not (first and t == 0)
                    if before:
                        copy_turned(n)
                    square(n, Q, t % 2)
                    square(n, K, t % 2)
                    if before:
                        hi_part(n, ip, tp, tp % 2)
                    if t == 0:
                        for h in range(HG):
                            silu_gate(i, h)

            iterations(act, run)
            n = TS * N
            copy_turned(n)
            hi_part(n, N - 1, TS - 1, 1)

        @block.gpsimd
        def _(pool):
            def run(i):
                for t in range(TS):
                    n, b = TS * i + t, t % 2
                    pool.wait_ge(guard_done, n + 1)
                    after(pool, q_scaled, n - 1)
                    after(pool, scale_done, n - 1)
                    pool.tensor_tensor(inv_norm[b][:, :], guarded[b][:, :], k.minus_half[:, :], ALU.pow)\
                        .then_inc(inverted, 1)
                    pool.wait_ge(inverted, n + 1)
                    q = heads(raw[Q][b][:, :])
                    pool.tensor_tensor(q, q, inv_norm[b][:, 0:HG].unsqueeze(2).broadcast_to([P, HG, P]), ALU.mult)\
                        .then_inc(q_scaled, 1)
                    after(pool, v_scaled, n - 1)
                    pool.tensor_tensor(v_scale[b][:, :], inv_norm[b][:, HG:2 * HG],
                                       k.beta[:, bass.ds(n % NT, 1), bass.ds((i // NS) * HG, HG)]
                                       .rearrange("p a h -> p (a h)"), ALU.mult).then_inc(scale_done, 1)
                    pool.wait_ge(scale_done, n + 1)
                    pool.wait_ge(biased[V], n + 1)
                    v = heads(raw[V][b][:, :])
                    pool.tensor_tensor(v, v, v_scale[b][:, :].unsqueeze(2).broadcast_to([P, HG, P]), ALU.mult)\
                        .then_inc(v_scaled, 1)

            iterations(pool, run)


def route_tokens(nc, x, ident, k, acc, x1, h_hi, h_lo, combine):
    ctx = ExitStack()
    with ctx:
        sb = lambda name, shape, dt=FP32: ctx.enter_context(nc.sbuf_tensor(name, shape, dt))
        pb = lambda name: ctx.enter_context(nc.psum_tensor(name, [P, 512], FP32))
        sem = lambda name: ctx.enter_context(nc.semaphore(name))
        x_in = [sb(f"r_x{b}", [P, TS, H]) for b in range(2)]
        delta = sb("r_delta", [P, KC, ST])
        stats, mean_var = sb("r_stats", [P, TS, 6]), sb("r_mean_var", [P, TS, 2])
        var_eps, rstd = sb("r_var_eps", [P, TS]), sb("r_rstd", [P, TS])
        xn = sb("r_xn", [P, TS, H])
        h_f = sb("r_h", [P, KC, ST])
        top, total = sb("r_top", [P, TS]), sb("r_total", [P, TS])
        prob, picked = sb("r_prob", [P, TS, E]), sb("r_picked", [P, TS, E])
        above, tied = sb("r_above", [P, TS, E, E]), sb("r_tied", [P, TS, E, E])
        rank = sb("r_rank", [P, TS, E])
        weights_t = sb("r_weights_t", [E, ST])
        delta_ps = [pb(f"r_delta_ps{j}") for j in range(2)]
        turned_ps = [pb(f"r_turned_ps{c}") for c in range(KC)]
        logit_ps, weight_ps, spread_ps = pb("r_logit_ps"), pb("r_weight_ps"), pb("r_spread_ps")
        loaded = [sem(f"r_loaded{b}") for b in range(2)]
        scaled, delta_turned, x1_done = sem("r_scaled"), sem("r_delta_turned"), sem("r_x1")
        stats_done, aggregated, eps_added, rstd_done = sem("r_st"), sem("r_ag"), sem("r_ep"), sem("r_rs")
        xn_done, turned, modulated, hi_done, lo_done = sem("r_xn"), sem("r_turned"), sem("r_mod"), sem("r_hi"), sem("r_lo")
        logits_done, shifted, exp_done, soft = sem("r_logits"), sem("r_shifted"), sem("r_exp"), sem("r_soft")
        weights_turned, weights_copied, spread_done, combined = (sem("r_wt"), sem("r_wc"), sem("r_spread"),
                                                                 sem("r_combined"))
        x_t = x.rearrange("b (a p) c -> (b a) p c", p=P)
        SOFT = 14
        block = ctx.enter_context(nc.Block())

        def supertiles(eng, run):
            for s in range(2):
                run(s, 0, s)
            with eng.Fori(1, NS // 2) as j:
                for b in range(2):
                    run(2 * j + b, j, b)

        @block.sync
        def _(sp):
            def load(s, use, b):
                after(sp, x1_done, s - 1)
                sp.dma_start(x_in[b][:, :, :], x_t[bass.ds(s * TS, TS)].rearrange("t p c -> p t c"))\
                  .then_inc(loaded[b], 16)

            supertiles(sp, load)

        @block.scalar
        def _(act):
            def weigh(s):
                act.wait_ge(shifted, s + 1)
                act.activation(prob[:, :, :], prob[:, :, :], ACT.Exp).then_inc(exp_done, 1)
                act.wait_ge(weights_turned, s + 1)
                after(act, spread_done, s)
                act.activation(weights_t[:, :], weight_ps[0:E, :], ACT.Copy).then_inc(weights_copied, 1)
                act.wait_ge(spread_done, s + 1)
                act.activation(combine[:, bass.ds(s * ST, ST)], spread_ps[:, :], ACT.Copy).then_inc(combined, 1)

            def run(s, use, b):
                after(act, delta_turned, s)
                for c in range(KC):
                    for j in range(BS):
                        at = s * BS + j
                        i = act.activation(delta[:, c, j * L:(j + 1) * L], acc[:, c, bass.ds(at * L, L)], ACT.Identity,
                                           bias=k.ga_ob[:, c, bass.ds(at, 1)],
                                           scale=k.mod[:, GA * KC + c, bass.ds(at, 1)])
                i.then_inc(scaled, 1)
                if not (isinstance(s, int) and s == 0):
                    weigh(s - 1)
                act.wait_ge(turned, s + 1)
                after(act, logits_done, s)
                after(act, lo_done, s)
                for c in range(KC):
                    for j in range(BS):
                        at = s * BS + j
                        i = act.activation(h_f[:, c, j * L:(j + 1) * L], turned_ps[c][:, j * L:(j + 1) * L],
                                           ACT.Identity, bias=k.mod[:, SB * KC + c, bass.ds(at, 1)],
                                           scale=k.mod[:, CB * KC + c, bass.ds(at, 1)])
                i.then_inc(modulated, 1)
                act.wait_ge(modulated, s + 1)
                act.activation(h_hi[:, :, bass.ds(s * ST, ST)], h_f[:, :, :], ACT.Copy).then_inc(hi_done, 1)

            supertiles(act, run)
            weigh(NS - 1)

        @block.tensor
        def _(pe):
            def weigh(s):
                pe.wait_ge(soft, SOFT * (s + 1))
                after(pe, weights_copied, s)
                for t in range(TS):
                    mm = pe.transpose(weight_ps[0:E, t * P:(t + 1) * P], picked[:, t, :], ident)
                mm.then_inc(weights_turned, 1)
                pe.wait_ge(weights_copied, s + 1)
                after(pe, combined, s)
                pe.matmul(spread_ps[:, :], k.spread[:, :], weights_t[:, :], start=True, stop=True).then_inc(spread_done, 1)

            def run(s, use, b):
                pe.wait_ge(scaled, s + 1)
                after(pe, x1_done, s)
                for t in range(TS):
                    for c in range(KC):
                        at = (t % 2) * H + c * P
                        mm = pe.transpose(delta_ps[t // 2][:, at:at + P], delta[:, c, t * P:(t + 1) * P], ident)
                mm.then_inc(delta_turned, 1)
                if not (isinstance(s, int) and s == 0):
                    weigh(s - 1)
                pe.wait_ge(xn_done, s + 1)
                after(pe, modulated, s)
                for c in range(KC):
                    for t in range(TS):
                        mm = pe.transpose(turned_ps[c][:, t * P:(t + 1) * P], xn[:, t, c * P:(c + 1) * P], ident)
                mm.then_inc(turned, 1)
                pe.wait_ge(modulated, s + 1)
                after(pe, shifted, s)
                for t in range(TS):
                    for c in range(KC):
                        mm = pe.matmul(logit_ps[:, t * E:(t + 1) * E], h_f[:, c, t * P:(t + 1) * P], k.gate_wt[:, c, :],
                                       start=(c == 0), stop=(c == KC - 1))
                mm.then_inc(logits_done, 1)

            supertiles(pe, run)
            weigh(NS - 1)

        @block.gpsimd
        def _(pool):
            def root(s, use, b):
                pool.wait_ge(eps_added, s + 1)
                after(pool, xn_done, s)
                pool.tensor_tensor(rstd[:, :], var_eps[:, :], k.minus_half[:, 0:TS], ALU.pow).then_inc(rstd_done, 1)

            supertiles(pool, root)

        @block.vector
        def _(dve):
            logits = logit_ps[:, 0:TS * E].rearrange("p (t e) -> p t e", e=E)

            def by_expert(v):
                return v[:, :].unsqueeze(2).broadcast_to([P, TS, E])

            def choose(s, x1_step, stats_step, aggr_step, eps_step):
                def done(n):
                    dve.wait_ge(soft, SOFT * s + n)

                dve.wait_ge(logits_done, s + 1)
                x1_step()
                dve.tensor_reduce(top[:, :], logits, AX.X, ALU.max).then_inc(soft, 1)
                stats_step()
                done(1)
                dve.tensor_tensor(prob[:, :, :], logits, by_expert(top), ALU.subtract).then_inc(shifted, 1)
                aggr_step()
                dve.wait_ge(exp_done, s + 1)
                dve.tensor_reduce(total[:, :], prob[:, :, :], AX.X, ALU.add).then_inc(soft, 1)
                eps_step()
                done(2)
                dve.reciprocal(total[:, :], total[:, :]).then_inc(soft, 1)
                done(3)
                dve.tensor_tensor(prob[:, :, :], prob[:, :, :], by_expert(total), ALU.mult).then_inc(soft, 1)
                other = prob[:, :, :].unsqueeze(2).broadcast_to([P, TS, E, E])
                own = prob[:, :, :].unsqueeze(3).broadcast_to([P, TS, E, E])
                tied_ef = tied[:, :, :, :].rearrange("p t e f -> p t (e f)")
                earlier = k.earlier[:, :, :].rearrange("p e f -> p (e f)").unsqueeze(1).broadcast_to([P, TS, E * E])
                done(4)
                dve.tensor_tensor(tied[:, :, :, :], other, own, ALU.is_equal).then_inc(soft, 1)
                dve.tensor_tensor(above[:, :, :, :], other, own, ALU.is_gt).then_inc(soft, 1)
                done(5)
                dve.tensor_tensor(tied_ef, tied_ef, earlier, ALU.mult).then_inc(soft, 1)
                done(7)
                dve.tensor_tensor(above[:, :, :, :], above[:, :, :, :], tied[:, :, :, :], ALU.add).then_inc(soft, 1)
                done(8)
                dve.tensor_reduce(rank[:, :, :], above[:, :, :, :], AX.X, ALU.add).then_inc(soft, 1)
                after(dve, weights_turned, s)
                done(9)
                dve.scalar_tensor_tensor(out=picked[:, :, :], in0=rank[:, :, :], scalar=float(TOPK),
                                         in1=prob[:, :, :], op0=ALU.is_lt, op1=ALU.mult).then_inc(soft, 1)
                done(10)
                dve.tensor_reduce(total[:, :], picked[:, :, :], AX.X, ALU.add).then_inc(soft, 1)
                done(11)
                dve.tensor_scalar(total[:, :], total[:, :], 1e-20, None, ALU.add).then_inc(soft, 1)
                done(12)
                dve.reciprocal(total[:, :], total[:, :]).then_inc(soft, 1)
                done(13)
                dve.tensor_tensor(picked[:, :, :], picked[:, :, :], by_expert(total), ALU.mult).then_inc(soft, 1)

            def add_residual(s, use, b):
                dve.wait_ge(delta_turned, s + 1)
                dve.wait_ge(loaded[b], 16 * (use + 1))
                for j in range(2):
                    i = dve.tensor_tensor(x1[:, bass.ds(s * TS + 2 * j, 2), :],
                                          delta_ps[j][:, :].rearrange("p (t c) -> p t c", t=2),
                                          x_in[b][:, 2 * j:2 * j + 2, :], ALU.add)
                i.then_inc(x1_done, 1)

            def measure(s):
                for t in range(TS):
                    i = dve.bn_stats(stats[:, t, :], x1[:, bass.ds(s * TS + t, 1), :].rearrange("p a c -> p (a c)"))
                i.then_inc(stats_done, 1)
                dve.wait_ge(stats_done, s + 1)

            def aggregate(s):
                for t in range(TS):
                    i = dve.bn_aggr(mean_var[:, t, :], stats[:, t, :])
                i.then_inc(aggregated, 1)

            def add_eps(s):
                dve.wait_ge(aggregated, s + 1)
                dve.tensor_scalar(var_eps[:, :], mean_var[:, :, 1], LN_EPS, None, ALU.add).then_inc(eps_added, 1)

            def normalize(s):
                dve.wait_ge(rstd_done, s + 1)
                after(dve, turned, s)
                for t in range(TS):
                    i = dve.tensor_scalar(xn[:, t, :], x1[:, bass.ds(s * TS + t, 1), :].rearrange("p a c -> p (a c)"),
                                          mean_var[:, t, 0:1], rstd[:, t:t + 1], ALU.subtract, ALU.mult)
                i.then_inc(xn_done, 1)
                dve.wait_ge(hi_done, s + 1)
                at = bass.ds(s * ST, ST)
                dve.tensor_tensor(h_lo[:, :, at], h_f[:, :, :], f32(h_hi[:, :, at]), ALU.subtract).then_inc(lo_done, 1)

            def run(s, use, b):
                add_residual(s, use, b)
                if isinstance(s, int) and s == 0:
                    dve.wait_ge(x1_done, 1)
                    measure(s)
                    aggregate(s)
                    add_eps(s)
                else:
                    choose(s - 1, lambda: dve.wait_ge(x1_done, s + 1), lambda: measure(s), lambda: aggregate(s),
                           lambda: add_eps(s))
                normalize(s)

            supertiles(dve, run)
            nothing = lambda: None
            choose(NS - 1, nothing, nothing, nothing, nothing)


def experts(nc, ident, k, tile_scr, h_hi, h_lo, combine, acc, x1, out):
    ctx = ExitStack()
    with ctx:
        sb = lambda name, shape, dt=FP32: ctx.enter_context(nc.sbuf_tensor(name, shape, dt))
        pb = lambda name: ctx.enter_context(nc.psum_tensor(name, [P, 512], FP32))
        sem = lambda name: ctx.enter_context(nc.semaphore(name))
        w = [sb(f"f_w{b}", [P, 2, MW], F32R) for b in range(4)]
        silu_g = [sb(f"f_silu{b}", [P, ST]) for b in range(2)]
        hid = [sb(f"f_hid{b}", [P, ST]) for b in range(2)]
        hid_hi = [sb(f"f_hid_hi{b}", [P, ST], F32R) for b in range(2)]
        hid_lo = [sb(f"f_hid_lo{b}", [P, ST], F32R) for b in range(2)]
        delta = [sb(f"f_delta{b}", [P, KC, ST]) for b in range(2)]
        res = [sb(f"f_res{b}", [P, TS, H]) for b in range(2)]
        g_ps = [pb(f"f_g_ps{b}") for b in range(2)]
        u_ps = [pb(f"f_u_ps{b}") for b in range(2)]
        y_ps = [pb(f"f_y_ps{c}") for c in range(KC)]
        w_loaded = [sem(f"f_w_loaded{b}") for b in range(4)]
        g_done, u_done = [sem(f"f_g{b}") for b in range(2)], [sem(f"f_u{b}") for b in range(2)]
        silu_done, weighted, hid_done = ([sem(f"f_silu_done{b}") for b in range(2)],
                                         [sem(f"f_weighted{b}") for b in range(2)],
                                         [sem(f"f_hid_done{b}") for b in range(2)])
        hi_done, lo_done = [sem(f"f_hi{b}") for b in range(2)], [sem(f"f_lo{b}") for b in range(2)]
        y_part = sem("f_y_part")
        y_done, added = [sem(f"f_y{c}") for c in range(KC)], [sem(f"f_added{c}") for c in range(KC)]
        scaled, turned, summed = sem("f_scaled"), sem("f_turned"), sem("f_summed")
        stored = [sem(f"f_stored{b}") for b in range(2)]
        out_t = out.rearrange("b (a p) c -> (b a) p c", p=P)
        PAIRS = -(-NM // 2)
        QUADS = (PAIRS - 3) // 2
        U = PAIRS * NS
        assert NM % 2 == 1 and ME == 2 * (PAIRS - 2) and 2 * QUADS + 3 == PAIRS

        def pairs(eng, run):
            run(0, 0, None)
            run(1, 2, 0)
            with eng.Fori(1, QUADS) as q:
                run(2 * q, 0, 2)
                run(2 * q + 1, 2, 0)
            for p in range(2 * QUADS, PAIRS):
                run(p, 2 * (p % 2), 2 - 2 * (p % 2))

        def is_last(p):
            return isinstance(p, int) and p == PAIRS - 1

        def is_shared(p):
            return isinstance(p, int) and p >= PAIRS - 2

        block = ctx.enter_context(nc.Block())

        @block.sync
        def _(sp):
            def load(m, b):
                sp.dma_start(f32(w[b][:, :, :]), tile_scr[bass.ds(m, 1)].rearrange("r p s n -> p (r s) n"))\
                  .then_inc(w_loaded[b], 16)

            for b in range(4):
                load(b, b)

            def reload(p, w0, _):
                sp.wait_ge(y_done[KC - 1], NS * (p + 1))
                for b in range(2):
                    if not (isinstance(p, int) and 2 * (p + 2) + b >= NM):
                        load(2 * (p + 2) + b, w0 + b)

            reload(0, 0, None)
            reload(1, 2, 0)
            with sp.Fori(1, QUADS) as q:
                reload(2 * q, 0, 2)
                reload(2 * q + 1, 2, 0)
            reload(PAIRS - 3, 0, 2)

            def store(s, b):
                sp.wait_ge(summed, s + 1)
                sp.dma_start(out_t[bass.ds(s * TS, TS)].rearrange("t p c -> p t c"), res[b][:, :, :])\
                  .then_inc(stored[b], 16)

            with sp.Fori(0, NS // 2) as j:
                for b in range(2):
                    store(2 * j + b, b)
            for b in range(2):
                sp.wait_ge(stored[b], 16 * (NS // 2))

        @block.tensor
        def _(pe):
            def up(p, u, s, w0, b):
                wb = w[w0 + b]
                if s is first_s:
                    pe.wait_ge(w_loaded[w0 + b], 16 * (p // 2 + 1))
                for what, ps, free, done in ((0, g_ps[b], silu_done[b], g_done[b]), (1, u_ps[b], hid_done[b], u_done[b])):
                    after(pe, free, u)
                    at = bass.ds(s * ST, ST)
                    for c in range(KC):
                        cols = slice(what * H + c * P, what * H + (c + 1) * P)
                        for m, (ws, x) in enumerate(((0, h_hi), (1, h_hi), (0, h_lo))):
                            mm = pe.matmul(ps[:, :], wb[:, ws, cols], x[:, c, at],
                                           start=(c == 0 and m == 0), stop=(c == KC - 1 and m == 2))
                    mm.then_inc(done, 1)

            def down(u, w0, b, alone=False):
                pe.wait_ge(hi_done[b], u + 1)
                wb = w[w0 + b]
                for c in range(KC):
                    if b == 0:
                        after(pe, added[c], u)
                    cols = slice(2 * H + c * P, 2 * H + (c + 1) * P)
                    for m, (ws, x) in enumerate(((0, hid_hi[b]), (1, hid_hi[b]), (0, hid_lo[b]))):
                        if c == 0 and m == 2:
                            pe.wait_ge(lo_done[b], u + 1)
                        last = m == 2 and (b == 1 or alone)
                        mm = pe.matmul(y_ps[c][:, :], wb[:, ws, cols], x[:, :], start=(b == 0 and m == 0), stop=last)
                    if b == 1 or alone:
                        mm.then_inc(y_done[c], 1)
                if b == 0 and not alone:
                    mm.then_inc(y_part, 1)

            first_s = 0

            def run(p, w0, w_before):
                def unit(s, w_last):
                    u = NS * p + s
                    up(p, u, s, w0, 0)
                    if w_last is not None:
                        down(u - 1, w_last, 1)
                    up(p, u, s, w0, 1)
                    down(u, w0, 0)

                if is_last(p):
                    def lone(s, w_last, b_last):
                        u = NS * p + s
                        up(p, u, s, w0, 0)
                        down(u - 1, w_last, b_last, alone=(b_last == 0))

                    lone(first_s, w_before, 1)
                    with pe.Fori(1, NS) as s:
                        lone(s, w0, 0)
                    down(U - 1, w0, 0, alone=True)
                    return
                unit(first_s, w_before)
                with pe.Fori(1, NS) as s:
                    unit(s, w0)

            pairs(pe, run)

            def turn(s, b):
                pe.wait_ge(scaled, s + 1)
                after(pe, summed, s - 1)
                for t in range(TS):
                    for c in range(KC):
                        at = (t % 2) * H + c * P
                        mm = pe.transpose((g_ps, u_ps)[t // 2][b][:, at:at + P], delta[b][:, c, t * P:(t + 1) * P],
                                          ident)
                mm.then_inc(turned, 1)

            turn(0, 0)
            turn(1, 1)
            with pe.Fori(1, NS // 2) as j:
                for b in range(2):
                    turn(2 * j + b, b)

        @block.scalar
        def _(act):
            def tile(p, u, b):
                act.wait_ge(g_done[b], u + 1)
                after(act, hid_done[b], u)
                act.activation(silu_g[b][:, :], g_ps[b][:, :], ACT.Silu).then_inc(silu_done[b], 1)

            def hi(u, b):
                act.wait_ge(hid_done[b], u + 1)
                if b == 0:
                    after(act, y_part, u)
                else:
                    after(act, y_done[KC - 1], u)
                act.activation(hid_hi[b][:, :], hid[b][:, :], ACT.Copy).then_inc(hi_done[b], 1)

            def run(p, w0, w_before):
                def unit(s):
                    u = NS * p + s
                    for b in range(1 if is_last(p) else 2):
                        tile(p, u, b)
                        if is_last(p):
                            act.wait_ge(y_part, NS * p)
                            after(act, y_done[KC - 1], u)
                            act.wait_ge(hid_done[b], u + 1)
                            act.activation(hid_hi[b][:, :], hid[b][:, :], ACT.Copy).then_inc(hi_done[b], 1)
                        else:
                            hi(u, b)

                with act.Fori(0, NS) as s:
                    unit(s)

            def first(p):
                for s in range(2):
                    u = NS * p + s
                    for b in range(2):
                        tile(p, u, b)
                        hi(u, b)
                with act.Fori(2, NS) as s:
                    for b in range(2):
                        tile(p, NS * p + s, b)
                        hi(NS * p + s, b)

            pairs(act, lambda p, w0, wb: first(p) if isinstance(p, int) and p == 0 else run(p, w0, wb))

            def scale(s, b):
                after(act, turned, s - 1)
                act.wait_ge(added[KC - 1], U)
                for c in range(KC):
                    for j in range(BS):
                        at = s * BS + j
                        i = act.activation(delta[b][:, c, j * L:(j + 1) * L], acc[:, c, bass.ds(at * L, L)], ACT.Copy,
                                           scale=k.mod[:, GB * KC + c, bass.ds(at, 1)])
                i.then_inc(scaled, 1)

            scale(0, 0)
            scale(1, 1)
            with act.Fori(1, NS // 2) as j:
                for b in range(2):
                    scale(2 * j + b, b)

        @block.vector
        def _(dve):
            def tile(p, u, s, b):
                dve.wait_ge(silu_done[b], u + 1)
                if is_shared(p):
                    a = silu_g[b]
                else:
                    a = silu_g[b]
                    dve.tensor_tensor(a[:, :], a[:, :], combine[:, bass.ds(s * ST, ST)], ALU.mult)\
                       .then_inc(weighted[b], 1)
                    dve.wait_ge(weighted[b], u + 1)
                dve.wait_ge(u_done[b], u + 1)
                after(dve, hi_done[b], u)
                after(dve, lo_done[b], u)
                dve.tensor_tensor(hid[b][:, :], u_ps[b][:, :], a[:, :], ALU.mult).then_inc(hid_done[b], 1)

            def lo(p, u, b):
                dve.wait_ge(hi_done[b], u + 1)
                dve.tensor_tensor(hid_lo[b][:, :], hid[b][:, :], f32(hid_hi[b][:, :]), ALU.subtract)\
                   .then_inc(lo_done[b], 1)

            def add(p, u, s):
                for c in range(KC):
                    dve.wait_ge(y_done[c], u + 1)
                    sums = acc[:, c, bass.ds(s * ST, ST)]
                    if isinstance(p, int) and p == 0:
                        i = dve.tensor_copy(sums, y_ps[c][:, :])
                    else:
                        i = dve.tensor_tensor(sums, y_ps[c][:, :], sums, ALU.add)
                    i.then_inc(added[c], 1)

            def run(p, w0, w_before):
                def unit(s, p_last, s_last):
                    u = NS * p + s
                    tile(p, u, s, 0)
                    lo(p, u, 0)
                    if p_last is not None:
                        add(p_last, u - 1, s_last)
                    if not is_last(p):
                        tile(p, u, s, 1)
                        lo(p, u, 1)

                if isinstance(p, int) and p == 0:
                    unit(0, None, None)
                    before = 0
                else:
                    unit(0, 0 if isinstance(p, int) and p == 1 else p - 1, NS - 1)
                with dve.Fori(1, NS) as s:
                    unit(s, p, s - 1)

            pairs(dve, run)
            add(PAIRS - 1, U - 1, NS - 1)

            def finish(s, b):
                dve.wait_ge(turned, s + 1)
                for j in range(2):
                    i = dve.tensor_tensor(res[b][:, 2 * j:2 * j + 2, :],
                                          (g_ps, u_ps)[j][b][:, :].rearrange("p (t c) -> p t c", t=2),
                                          x1[:, bass.ds(s * TS + 2 * j, 2), :], ALU.add)
                i.then_inc(summed, 1)

            finish(0, 0)
            finish(1, 1)
            with dve.Fori(1, NS // 2) as j:
                for b in range(2):
                    dve.wait_ge(stored[b], 16 * j)
                    finish(2 * j + b, b)


class Kept:
    pass


def build(nc, x, q_w, q_b, k_w, k_b, v_w, v_b, b_w, b_b, og_w, o_w, o_b, gate_w, w13, w2, sw13, sw2, c, wmod, out):
    ctx = ExitStack()
    with ctx:
        sb = lambda name, shape, dt=FP32: ctx.enter_context(nc.sbuf_tensor(name, shape, dt))
        dram = lambda name, shape: nc.dram_tensor(name, shape, FP32, kind="Internal").ap()
        ident = sb("ident", [P, P])
        k = Kept()
        k.mod = sb("mod", [P, 6 * KC, B])
        k.sign = sb("sign", [P, KC, B])
        k.ga_ob = sb("ga_ob", [P, KC, B])
        k.o_b = sb("o_b_sb", [P, KC])
        k.b_b = sb("b_b_sb", [P, NH])
        k.b_wt = sb("b_wt", [P, KC, NH])
        k.gate_wt = sb("gate_wt", [P, KC, E])
        k.beta = sb("beta", [P, NT, NH])
        k.minus_half = sb("minus_half", [P, 2 * HG])
        k.causal = sb("causal", [P, P])
        k.earlier = sb("earlier", [P, E, E])
        k.spread = sb("spread", [E, P])
        head_scr = dram("head_scr", (NH, 2, P, HW_))
        tile_scr = dram("tile_scr", (NM, P, 2, MW))
        h_scr = dram("h_scr", (NT, P, 2 * KC * P))
        made = ctx.enter_context(nc.semaphore("constants_made"))
        with nc.Block() as block:
            @block.gpsimd
            def _(pool):
                pool.memset(ident[:, :], 0.0)
                pool.memset(k.minus_half[:, :], -0.5)
                pool.memset(k.causal[:, :], 1.0)
                pool.memset(k.earlier[:, :, :], 1.0)
                pool.memset(k.spread[:, :], 1.0).then_inc(made, 1)
                pool.wait_ge(made, 1)
                pool.affine_select(out=ident[:, :], in_=ident[:, :], compare_op=ALU.not_equal, fill=1.0, base=0,
                                   pattern=[[-1, P]], channel_multiplier=1)
                pool.affine_select(out=k.causal[:, :], in_=k.causal[:, :], compare_op=ALU.is_ge, fill=0.0, base=0,
                                   pattern=[[1, P]], channel_multiplier=-1)
                pool.affine_select(out=k.earlier[:, :, :], in_=k.earlier[:, :, :], compare_op=ALU.is_ge, fill=0.0,
                                   base=-1, pattern=[[1, E], [-1, E]], channel_multiplier=0)
                pool.affine_select(out=k.spread[:, :], in_=k.spread[:, :], compare_op=ALU.is_ge, fill=0.0, base=0,
                                   pattern=[[1, P]], channel_multiplier=-ER).then_inc(made, 1)
                pool.wait_ge(made, 2)
                pool.affine_select(out=k.spread[:, :], in_=k.spread[:, :], compare_op=ALU.is_ge, fill=0.0,
                                   base=ER - 1, pattern=[[-1, P]], channel_multiplier=ER)
                pool.memset(k.causal[0:CH, CH:P], 0.0).then_inc(made, 1)
                pool.wait_ge(made, 3)
        prepare_weights(nc, q_w, k_w, v_w, og_w, o_w, w13, w2, sw13, sw2, ident[:, :], head_scr, tile_scr)
        modulation(nc, c, wmod, o_b, b_w, gate_w, b_b, ident[:, :], k)
        normalize_inputs(nc, x, ident[:, :], k, h_scr)
        acc = sb("acc", [P, KC, T])
        attention(nc, q_b, k_b, v_b, ident[:, :], k, head_scr, h_scr, acc)
        x1 = sb("x1", [P, NT, H])
        h_hi, h_lo = sb("h_hi", [P, KC, T], F32R), sb("h_lo", [P, KC, T], F32R)
        combine = sb("combine", [P, T])
        route_tokens(nc, x, ident[:, :], k, acc, x1, h_hi, h_lo, combine)
        experts(nc, ident[:, :], k, tile_scr, h_hi, h_lo, combine, acc, x1, out)


_INS = ['L0_attn_hidden_states', 'L0_attn_q_w', 'L0_attn_q_b', 'L0_attn_k_w', 'L0_attn_k_b', 'L0_attn_v_w',
        'L0_attn_v_b', 'L0_attn_b_w', 'L0_attn_b_b', 'L0_attn_og_w', 'L0_attn_o_w', 'L0_attn_o_b',
        'L0_ffn_gate_w', 'L0_ffn_w13', 'L0_ffn_w2', 'L0_ffn_sw13', 'L0_ffn_sw2', 'L0_c', 'L0_wmod']


def kernel(**inputs):
    import numpy as _np
    import concourse.bacc as _bacc
    from concourse import mybir as _mybir
    from concourse.bass_utils import run_bass_kernel_spmd as _run

    nc = _bacc.Bacc("TRN2", target_bir_lowering=False, num_devices=1)
    arrays, args = {}, []
    for name in _INS:
        a = _np.ascontiguousarray(inputs[name])
        arrays[f"in_{name}_dram"] = a
        args.append(nc.dram_tensor(f"in_{name}_dram", a.shape, _mybir.dt.from_np(a.dtype), kind="ExternalInput").ap())
    out = nc.dram_tensor("out_dram", (B, L, H), _mybir.dt.float32, kind="ExternalOutput").ap()
    build(nc, *args, out)
    r = _run(nc, [arrays], core_ids=[0])
    return r.results[0]["out_dram"]
```
